# Optimizing a Trainium2 kernel written in Bass

```python
import numpy as np
import jax
import jax.numpy as jnp

def _softmax(x, axis=-1):
    return jax.nn.softmax(x, axis=axis)

def _gelu(x):
    return jax.nn.gelu(x, approximate=True)

def _silu(x):
    return jax.nn.silu(x)

def _sigmoid(x):
    return jax.nn.sigmoid(x)

def _layernorm(x, axis=-1, eps=1e-05):
    m = jnp.mean(x, axis=axis, keepdims=True)
    v = jnp.var(x, axis=axis, keepdims=True)
    return (x - m) / jnp.sqrt(v + eps)

def _scatter_add(tgt, idx, src, axis=0):
    return tgt.at[idx].add(src)

def _segment_sum(src, seg, n):
    return jax.ops.segment_sum(src, seg, n)
kernel_name = 'mk_seq_postln_d1_jaxref_r8_14a54f'

def setup_inputs(seed: int=0):
    np.random.seed(seed)
    _w = jnp.asarray

    def _L0_attn_setup():
        import jax, jax.numpy as jnp
        import numpy as np
        HIDDEN = 512
        NUM_HEADS = 32
        NUM_KV_HEADS = 8
        HEAD_DIM = 128
        key = jax.random.key(seed)
        k0, k1, k2, k3, k4 = jax.random.split(key, 5)
        B, S = (1, 256)
        s = 0.02
        return {'hidden_states': jax.random.normal(k0, (B, S, HIDDEN), dtype=jnp.float32), 'Wq': jax.random.normal(k1, (HIDDEN, NUM_HEADS * HEAD_DIM), dtype=jnp.float32) * s, 'Wk': jax.random.normal(k2, (HIDDEN, NUM_KV_HEADS * HEAD_DIM), dtype=jnp.float32) * s, 'Wv': jax.random.normal(k3, (HIDDEN, NUM_KV_HEADS * HEAD_DIM), dtype=jnp.float32) * s, 'Wo': jax.random.normal(k4, (NUM_HEADS * HEAD_DIM, HIDDEN), dtype=jnp.float32) * s}
    _L0_attn_in = _L0_attn_setup()

    def _L0_ffn_setup():
        import jax, jax.numpy as jnp
        import numpy as np

        def sparsemax(z):
            E = z.shape[-1]
            z_sorted = -jnp.sort(-z, axis=-1)
            z_cum = jnp.cumsum(z_sorted, axis=-1)
            k = jnp.arange(1, E + 1, dtype=z.dtype)
            support = 1.0 + k * z_sorted > z_cum
            k_z = jnp.sum(support, axis=-1, keepdims=True)
            tau_sum = jnp.take_along_axis(z_cum, k_z.astype(jnp.int32) - 1, axis=-1)
            tau = (tau_sum - 1.0) / k_z.astype(z.dtype)
            return jnp.maximum(z - tau, 0.0)
        key = jax.random.key(seed)
        ks = jax.random.split(key, 6)
        B, S, D_IN, D_OUT, E, R = (8, 256, 512, 512, 8, 16)
        x = jax.random.normal(ks[0], (B, S, D_IN), dtype=jnp.float32)
        W_base = jax.random.normal(ks[1], (D_OUT, D_IN), dtype=jnp.float32) * D_IN ** (-0.5)
        b_base = jax.random.normal(ks[2], (D_OUT,), dtype=jnp.float32) * 0.01
        W_router = jax.random.normal(ks[3], (E, D_IN), dtype=jnp.float32) * D_IN ** (-0.5)
        b_router = jnp.zeros((E,), dtype=jnp.float32)
        lora_A = jax.random.normal(ks[4], (E, D_IN, R), dtype=jnp.float32) * D_IN ** (-0.5)
        lora_B = jnp.zeros((E, R, D_OUT), dtype=jnp.float32)
        return {'x': x, 'W_base': W_base, 'b_base': b_base, 'W_router': W_router, 'b_router': b_router, 'lora_A': lora_A, 'lora_B': lora_B}
    _L0_ffn_in = _L0_ffn_setup()
    _d = {'L0_attn_hidden_states': _L0_attn_in['hidden_states'], 'L0_attn_Wq': _L0_attn_in['Wq'], 'L0_attn_Wk': _L0_attn_in['Wk'], 'L0_attn_Wv': _L0_attn_in['Wv'], 'L0_attn_Wo': _L0_attn_in['Wo'], 'L0_ffn_W_base': _L0_ffn_in['W_base'], 'L0_ffn_b_base': _L0_ffn_in['b_base'], 'L0_ffn_W_router': _L0_ffn_in['W_router'], 'L0_ffn_b_router': _L0_ffn_in['b_router'], 'L0_ffn_lora_A': _L0_ffn_in['lora_A'], 'L0_ffn_lora_B': _L0_ffn_in['lora_B']}
    _x0 = _d['L0_attn_hidden_states']
    _d['L0_attn_hidden_states'] = jax.random.normal(jax.random.fold_in(jax.random.key(seed), 1), (2, 512, 512), dtype=_x0.dtype)
    del _x0
    return _d

def reference(L0_attn_hidden_states, L0_attn_Wq, L0_attn_Wk, L0_attn_Wv, L0_attn_Wo, L0_ffn_W_base, L0_ffn_b_base, L0_ffn_W_router, L0_ffn_b_router, L0_ffn_lora_A, L0_ffn_lora_B):

    def _L0_attn_ref(hidden_states, Wq, Wk, Wv, Wo):
        import jax, jax.numpy as jnp
        import numpy as np
        HIDDEN = 512
        NUM_HEADS = 32
        NUM_KV_HEADS = 8
        HEAD_DIM = 128
        B, S, _ = hidden_states.shape
        n_rep = NUM_HEADS // NUM_KV_HEADS
        q = (hidden_states @ Wq).reshape(B, S, NUM_HEADS, HEAD_DIM).transpose(0, 2, 1, 3)
        k = (hidden_states @ Wk).reshape(B, S, NUM_KV_HEADS, HEAD_DIM).transpose(0, 2, 1, 3)
        v = (hidden_states @ Wv).reshape(B, S, NUM_KV_HEADS, HEAD_DIM).transpose(0, 2, 1, 3)
        k = jnp.repeat(k, n_rep, axis=1)
        v = jnp.repeat(v, n_rep, axis=1)
        scale = HEAD_DIM ** (-0.5)
        scores = jnp.einsum('bhqd,bhkd->bhqk', q, k) * scale
        causal = jnp.tril(jnp.ones((S, S), dtype=bool))
        scores = jnp.where(causal[None, None], scores, jnp.float32(-jnp.inf))
        probs = jax.nn.softmax(scores, axis=-1)
        out = jnp.einsum('bhqk,bhkd->bhqd', probs, v)
        out = out.transpose(0, 2, 1, 3).reshape(B, S, NUM_HEADS * HEAD_DIM)
        return out @ Wo

    def _L0_ffn_ref(x, W_base, b_base, W_router, b_router, lora_A, lora_B):
        import jax, jax.numpy as jnp
        import numpy as np

        def sparsemax(z):
            E = z.shape[-1]
            z_sorted = -jnp.sort(-z, axis=-1)
            z_cum = jnp.cumsum(z_sorted, axis=-1)
            k = jnp.arange(1, E + 1, dtype=z.dtype)
            support = 1.0 + k * z_sorted > z_cum
            k_z = jnp.sum(support, axis=-1, keepdims=True)
            tau_sum = jnp.take_along_axis(z_cum, k_z.astype(jnp.int32) - 1, axis=-1)
            tau = (tau_sum - 1.0) / k_z.astype(z.dtype)
            return jnp.maximum(z - tau, 0.0)
        base_out = jnp.einsum('bsd,od->bso', x, W_base) + b_base
        logits = jnp.einsum('bsd,ed->bse', x, W_router) + b_router
        weights = sparsemax(logits)
        h = jnp.einsum('bsd,edr->bser', x, lora_A)
        expert_out = jnp.einsum('bser,bse,ero->bso', h, weights, lora_B)
        return base_out + expert_out
    x = L0_attn_hidden_states
    x = _layernorm(x + _L0_attn_ref(x, L0_attn_Wq, L0_attn_Wk, L0_attn_Wv, L0_attn_Wo), axis=-1)
    x = _layernorm(x + _L0_ffn_ref(x, L0_ffn_W_base, L0_ffn_b_base, L0_ffn_W_router, L0_ffn_b_router, L0_ffn_lora_A, L0_ffn_lora_B), axis=-1)
    return x

_drawn_inputs = setup_inputs


def setup_inputs(seed=0):
    import zlib

    import numpy as np

    out = dict(_drawn_inputs(seed))
    spreads = {'L0_ffn_b_router': (0.0, 0.525), 'L0_ffn_lora_B': (0.0, 0.1)}
    factors = {'L0_attn_Wq': 4.558, 'L0_attn_Wk': 4.49, 'L0_ffn_b_base': 8.0}
    for name, (base, spread) in spreads.items():
        noise = np.random.default_rng([zlib.crc32(name.encode()), seed]).standard_normal(out[name].shape)
        drawn = base * np.exp(spread * noise) if base else spread * noise
        out[name] = jnp.asarray(drawn.astype(out[name].dtype))
    for name, factor in factors.items():
        out[name] = (out[name] * factor).astype(out[name].dtype)
    return out
```

```python
import numpy as np
import concourse.bass as bass
from concourse import mybir
from contextlib import ExitStack


def post_ln_block(nc, xT_d, x_d, wq_d, wk_d, wv_d, wo_d, wb_d, wra_d, lb_d, bb_d, br_d, out_d):
    f32, f32r = mybir.dt.float32, mybir.dt.float32r
    ALU, ACT = mybir.AluOpType, mybir.ActivationFunctionType

    G, B, NI, HG, C = 8, 2, 4, 4, 4
    NU, NT = G * B, G * B * NI
    SCALE = 128.0 ** -0.5
    EPS = 1e-5
    NRAW, NWO, NV, NPT = 6, 6, 12, 4
    BIG = 3.0e38

    ctx = ExitStack()
    with ctx:
        def sb(name, shape, dt=f32):
            return ctx.enter_context(nc.sbuf_tensor(name, shape, dt))

        def sem(name):
            return ctx.enter_context(nc.semaphore(name))

        raw = sb("raw", [128, NRAW, 544])
        xT = [sb("xT_hi", [128, C, 1024], f32r), sb("xT_lo", [128, C, 1024], f32r)]
        wq = [sb("wq_hi", [128, HG, 512], f32r), sb("wq_lo", [128, HG, 512], f32r)]
        wk = [sb("wk_hi", [128, 512], f32r), sb("wk_lo", [128, 512], f32r)]
        wv = [sb("wv_hi", [128, 1024], f32r), sb("wv_lo", [128, 1024], f32r)]
        wo = [sb("wo_hi", [128, NWO, 512], f32r), sb("wo_lo", [128, NWO, 512], f32r)]
        kT = [sb("kT_hi", [128, 512], f32r), sb("kT_lo", [128, 512], f32r)]
        qT = [sb("qT_hi", [128, HG, 512], f32r), sb("qT_lo", [128, HG, 512], f32r)]
        v = [sb("v_hi", [128, NV, 256], f32r), sb("v_lo", [128, NV, 256], f32r)]
        pr = sb("pr", [128, 8, 512])
        pT = [sb("pT_hi", [128, NPT, 512], f32r), sb("pT_lo", [128, NPT, 512], f32r)]
        oT = [sb("oT_hi", [128, 2, 512], f32r), sb("oT_lo", [128, 2, 512], f32r)]
        y = sb("y", [128, 8, 512])
        mask = sb("mask", [128, 512])
        ident = sb("ident", [128, 128])
        mx = sb("mx", [128, 8])
        rs = sb("rs", [128, 8])
        ri = sb("ri", [128, 8])
        bb = sb("bb", [128, 512])
        br = sb("br", [128, 8])
        kk = sb("kk", [128, 8])
        ones8 = sb("ones8", [128, 8])
        mhalf = sb("mhalf", [128, 1])
        st = sb("st", [128, 4, 6])
        mv = sb("mv", [128, 4, 2])
        vs = sb("vs", [128, 4])
        rstd = sb("rstd", [128, 4])
        sp = sb("sp", [128, 2, 64])
        hw = sb("hw", [128, 2, 128])
        hwT = [sb("hwT_hi", [128, 2, 128], f32r), sb("hwT_lo", [128, 2, 128], f32r)]
        zT = [wq[0], wq[1]]
        wb = [x[:, 0:2, :].rearrange("p a n -> p (a n)") for x in xT]
        wra = [x[:, 2, 0:544] for x in xT]
        lb = [x[:, 3, 0:512] for x in xT]

        bank = [ctx.enter_context(nc.psum_tensor(f"bank{n}", [128, 512], f32)) for n in range(8)]
        S_BANKS, T_BANKS, A_BANKS = bank[0:3], bank[3:5], bank[5:8]

        sems = {e: sem(f"s_{e}") for e in ("pe", "act", "dve", "pool")}
        s_raw = [sem(f"s_raw{n}") for n in range(NRAW)]
        s_x, s_b, s_out = sem("s_x"), sem("s_b"), sem("s_out")
        sems.update({f"raw{n}": s for n, s in enumerate(s_raw)})
        sems.update(x=s_x, b=s_b, out=s_out)

        queue = {e: [] for e in ("pe", "act", "dve", "pool", "sp")}
        count = {}
        at = {}

        def op(engine, fn, waits=(), mark=None, dma=None):
            name = dma or engine
            found = [at[w] for w in waits]
            by = 0
            if mark is not None:
                by = 16 if dma else 1
                count[name] = count.get(name, 0) + by
                at[mark] = (name, count[name])
            queue[engine].append((found, fn, name, by))

        def play(engine, eng):
            seen = {}
            for found, fn, name, by in queue[engine]:
                for s, n in found:
                    if seen.get(s, 0) < n:
                        eng.wait_ge(sems[s], n)
                        seen[s] = n
                ins = fn(eng)
                if by:
                    ins.then_inc(sems[name], by)

        def raw_of(t):
            return t.bitcast(f32)

        free = {"S": [(x, []) for x in S_BANKS], "T": [(x, []) for x in T_BANKS], "A": [(x, []) for x in A_BANKS]}

        def take(kind):
            out, before = free[kind].pop(0)
            return out, (kind, out), before

        def give(place, mark):
            free[place[0]].append((place[1], [mark]))

        def passes(out, pairs, waits, mark, first=True, last=True):
            todo = [(a[i], b[j]) for a, b in pairs for i, j in ((0, 0), (0, 1), (1, 0))]
            for n, (a, b) in enumerate(todo):
                op("pe", lambda e, a=a, b=b, s=first and n == 0, t=last and n == len(todo) - 1:
                   e.matmul(out, a, b, start=s, stop=t),
                   waits if n == 0 else (), mark if n == len(todo) - 1 else None)

        def split(src, hi, lo, name, waits, hi_engine="act", lo_engine="dve"):
            if hi_engine == "act":
                op("act", lambda e: e.activation(hi, src, ACT.Copy), waits, ("hi",) + name)
            else:
                op(hi_engine, lambda e: e.tensor_copy(hi, src), waits, ("hi",) + name)
            op(lo_engine, lambda e: e.tensor_tensor(out=lo, in0=src, in1=raw_of(hi), op=ALU.subtract),
               [("hi",) + name], ("lo",) + name)

        pieces = [0]

        def piece(name, src, dst, cols=512, shape=None, after=(), lo_engine="pool", hi_engine="act"):
            n = pieces[0]
            pieces[0] += 1
            slot = n % NRAW
            r = raw[:, slot, 0:cols]
            rv = r.rearrange("p (c n) -> p c n", c=shape) if shape else r
            op("sp", lambda e: e.dma_start(rv, src), [("piece", n - NRAW)] if n >= NRAW else [],
               ("raw", n), dma=f"raw{slot}")
            split(r if cols == dst[0].shape[-1] else rv, dst[0], dst[1], name, [("raw", n), *after],
                  hi_engine, lo_engine)
            at["piece", n] = at[("lo",) + name]

        wq_v = wq_d.rearrange("(c p) n -> p c n", p=128)
        wk_v = wk_d.rearrange("(c p) n -> p c n", p=128)
        wv_v = wv_d.rearrange("(c p) n -> p c n", p=128)
        wo_v = wo_d.rearrange("(h p) n -> p h n", p=128)
        xT_v = xT_d.rearrange("(c p) t -> p c t", p=128)
        wb_v = wb_d.rearrange("(c p) n -> p c n", p=128)
        wra_v = wra_d.rearrange("(c p) n -> p c n", p=128)

        def load_x(b, c, lo_engine):
            piece(("x", b, c), xT_v[:, c, b * 512:(b + 1) * 512],
                  [t[:, c, b * 512:(b + 1) * 512] for t in xT], lo_engine=lo_engine)

        def load_wk(g, lo_engine="pool"):
            piece(("wk", g), wk_v[:, :, g * 128:(g + 1) * 128], [t[:, :] for t in wk], shape=C,
                  after=[("K", 2 * g - 1)] if g else [], lo_engine=lo_engine)

        def load_wq(g, h, lo_engine="pool"):
            n = HG * g + h
            piece(("wq", g, h), wq_v[:, :, n * 128:(n + 1) * 128], [t[:, h, :] for t in wq], shape=C,
                  after=[("Q", 2 * g - 1, h)] if g else [], lo_engine=lo_engine)

        def load_wo(g, h, lo_engine="pool"):
            n = HG * g + h
            old = (n - NWO) // HG
            piece(("wo", g, h), wo_v[:, n, :], [t[:, n % NWO, :] for t in wo],
                  after=[("W", 8 * old + 7)] if n >= NWO else [], lo_engine=lo_engine)

        def load_wv(p, k, lo_engine="pool"):
            piece(("wv", p, k), wv_v[:, 2 * k:2 * k + 2, p * 256:(p + 1) * 256],
                  [t[:, k * 512:(k + 1) * 512] for t in wv], shape=2,
                  after=[("Vp", p - 1, 7)] if p else [], lo_engine=lo_engine)

        def x_of(b):
            return [("lo", "x", b, c) for c in range(C)]

        def project_k(u):
            g, b = divmod(u, B)
            out, n, before = take("A")
            passes(out[:, :], [([t[:, c * 128:(c + 1) * 128] for t in wk],
                                [t[:, c, b * 512:(b + 1) * 512] for t in xT]) for c in range(C)],
                   before + [("lo", "wk", g)] + x_of(b), ("K", u))
            split(out[:, :], kT[0][:, :], kT[1][:, :], ("kT", u),
                  [("K", u)] + ([("S", 4 * u - 1, HG - 1)] if u else []))
            give(n, ("lo", "kT", u))

        def project_q(u, h):
            g, b = divmod(u, B)
            out, n, before = take("A")
            passes(out[:, :], [([t[:, h, c * 128:(c + 1) * 128] for t in wq],
                                [t[:, c, b * 512:(b + 1) * 512] for t in xT]) for c in range(C)],
                   before + [("lo", "wq", g, h)] + x_of(b), ("Q", u, h))
            split(out[:, :], qT[0][:, h, :], qT[1][:, h, :], ("qT", u, h),
                  [("Q", u, h)] + ([("S", 4 * u - 1, h)] if u else []))
            give(n, ("lo", "qT", u, h))

        def v_slot(p, tt):
            return (8 * p + tt) % NV

        def project_v(p, tt):
            out, n, before = take("A")
            old = 8 * p + tt - NV
            after = []
            if old >= 0:
                op_, ot = divmod(old, 8)
                after = [("V", 4 * (2 * (2 * op_ + 1) + ot // 4) + 3, 3)]
            passes(out[:, 0:256], [([t[:, c, tt * 128:(tt + 1) * 128] for t in xT],
                                    [t[:, c * 256:(c + 1) * 256] for t in wv]) for c in range(C)],
                   before + [("lo", "wv", p, 0), ("lo", "wv", p, 1)] + x_of(tt // 4), ("Vp", p, tt))
            s = v_slot(p, tt)
            split(out[:, 0:256], v[0][:, s, :], v[1][:, s, :], ("v", p, tt), [("Vp", p, tt)] + after)
            give(n, ("lo", "v", p, tt))

        def scores(t):
            u, i = divmod(t, NI)
            w = 128 * (i + 1)
            for h in range(HG):
                out, n, before = take("S")
                passes(out[:, 0:w], [([x[:, h, i * 128:(i + 1) * 128] for x in qT],
                                      [x[:, 0:w] for x in kT])],
                       before + [("lo", "qT", u, h), ("lo", "kT", u)], ("S", t, h))
                k = 4 * (t % 2) + h
                op("dve", lambda e, out=out, k=k: e.tensor_tensor_reduce(
                    out=pr[:, k, 0:w], in0=out[:, 0:w], in1=mask[:, 512 - w:512], scale=-SCALE, scalar=BIG,
                    op0=ALU.add, op1=ALU.min, accum_out=mx[:, k:k + 1]),
                   [("S", t, h), "mask"] + ([("T", t - 2, (t - 2) % NI)] if t >= 2 else []), ("max", t, h))
                give(n, ("max", t, h))
                op("act", lambda e, k=k: e.activation(
                    pr[:, k, 0:w], pr[:, k, 0:w], ACT.Exp, bias=mx[:, k:k + 1], scale=-1.0,
                    accum_out=rs[:, k:k + 1]), [("max", t, h)], ("exp", t, h))

        def normalise(t):
            w = 128 * (t % NI + 1)
            k0 = 4 * (t % 2)
            op("dve", lambda e: e.reciprocal(ri[:, k0:k0 + 4], rs[:, k0:k0 + 4]), [("exp", t, HG - 1)],
               ("ri", t))
            for h in range(HG):
                k = k0 + h
                p = pr[:, k, 0:w]
                if h < 2:
                    op("pool", lambda e, p=p, k=k: e.tensor_tensor(
                        out=p, in0=p, in1=ri[:, k:k + 1].to_broadcast([128, w]), op=ALU.mult),
                       [("ri", t)], ("p", t, h))
                else:
                    op("dve", lambda e, p=p, k=k: e.tensor_scalar(p, p, ri[:, k:k + 1], None, ALU.mult),
                       [("ri", t)], ("p", t, h))

        pt_at, pt_n = {}, [0]

        def turn(t, j):
            out, n, before = take("T")
            for h in range(HG):
                op("pe", lambda e, h=h: e.transpose(out[:, h * 128:(h + 1) * 128],
                                                    pr[:, 4 * (t % 2) + h, j * 128:(j + 1) * 128], ident[:, :]),
                   (before + ["ident"] if h == 0 else []) + [("p", t, h)], ("T", t, j) if h == HG - 1 else None)
            s = pt_n[0]
            pt_n[0] += 1
            pt_at[s] = (t, j)
            split(out[:, :], pT[0][:, s % NPT, :], pT[1][:, s % NPT, :], ("pT", t, j),
                  [("T", t, j)] + ([("V", *pt_at[s - NPT])] if s >= NPT else []))
            pt_at[t, j] = s % NPT
            give(n, ("lo", "pT", t, j))

        pv_bank = {}

        def weigh(t, j):
            u, i = divmod(t, NI)
            g, b = divmod(u, B)
            if j == 0:
                pv_bank[t] = take("A")
            out, n, before = pv_bank[t]
            s, k = v_slot(g // 2, 4 * b + j), pt_at[t, j]
            cols = slice((g % 2) * 128, (g % 2) * 128 + 128)
            passes(out[:, :], [([x[:, s, cols] for x in v], [x[:, k, :] for x in pT])],
                   (before if j == 0 else []) + [("lo", "pT", t, j), ("lo", "v", g // 2, 4 * b + j)],
                   ("V", t, j), j == 0, j == i)
            if j == i:
                split(out[:, :], oT[0][:, t % 2, :], oT[1][:, t % 2, :], ("oT", t),
                      [("V", t, i)] + ([("W", t - 2)] if t >= 2 else []))
                give(n, ("lo", "oT", t))

        wo_bank = {}

        def out_proj(t, h):
            u, i = divmod(t, NI)
            g, b = divmod(u, B)
            if h == 0:
                wo_bank[t] = take("A")
            out, n, before = wo_bank[t]
            s = (HG * g + h) % NWO
            passes(out[:, :], [([x[:, t % 2, h * 128:(h + 1) * 128] for x in oT], [x[:, s, :] for x in wo])],
                   (before if h == 0 else []) + [("lo", "oT", t), ("lo", "wo", g, h)],
                   ("W", t) if h == HG - 1 else None, h == 0, h == HG - 1)
            if h == HG - 1:
                k = 4 * b + i
                op("dve", lambda e: e.tensor_tensor(out=y[:, k, :], in0=out[:, :], in1=y[:, k, :], op=ALU.add),
                   [("W", t), ("y", g - 1, k) if g else "x"], ("y", g, k))
                give(n, ("y", g, k))

        def norm_of(src, dst, k, name, waits):
            n = name[1] % 2 + (2 if name[0] == "ln2" else 0)
            op("dve", lambda e: e.bn_stats(st[:, n, :], src), waits, name + ("st",))
            op("dve", lambda e: e.bn_aggr(mv[:, n, :], st[:, n, :]), [name + ("st",)], name + ("mv",))
            op("pool", lambda e: e.tensor_scalar(vs[:, n:n + 1], mv[:, n, 1:2], EPS, None, ALU.add),
               [name + ("mv",)], name + ("vs",))
            op("pool", lambda e: e.tensor_tensor(out=rstd[:, n:n + 1], in0=vs[:, n:n + 1], in1=mhalf[:, :],
                                                 op=ALU.pow), [name + ("vs",), "mhalf"], name + ("rstd",))
            op("dve", lambda e: e.tensor_scalar(dst, src, mv[:, n, 0:1], rstd[:, n:n + 1], ALU.subtract, ALU.mult),
               [name + ("rstd",)], name)

        def ffn_norm(k):
            norm_of(y[:, k, :], y[:, k, :], k, ("ln1", k), [("y", G - 1, k)])

        def ffn_turn(k):
            out, n, before = take("T")
            for c in range(C):
                op("pe", lambda e, c=c: e.transpose(out[:, c * 128:(c + 1) * 128], y[:, k, c * 128:(c + 1) * 128],
                                                    ident[:, :]),
                   before + [("ln1", k)] if c == 0 else (), ("zt", k) if c == C - 1 else None)
            after = [("RA", k - 2)] if k >= 2 else [("Q", NU - 1, HG - 1)]
            split(out[:, :], zT[0][:, k % 2, :], zT[1][:, k % 2, :], ("zT", k), [("zt", k)] + after)
            give(n, ("lo", "zT", k))
            op("pool", lambda e: e.tensor_tensor(out=y[:, k, :], in0=y[:, k, :], in1=bb[:, :], op=ALU.add),
               [("zt", k), "bias"], ("zb", k))

        ffn_bank = {}

        def ffn_products(k):
            ffn_bank[k] = take("A")
            base, _, before = ffn_bank[k]
            lhs = [[t[:, k % 2, c * 128:(c + 1) * 128] for t in zT] for c in range(C)]
            ra, n, before_ra = take("S")
            passes(ra[:, 0:136], [(lhs[c], [t[:, c * 136:(c + 1) * 136] for t in wra]) for c in range(C)],
                   before_ra + [("lo", "zT", k), ("lo", "wra")], ("R", k))
            passes(base[:, :], [(lhs[c], [t[:, c * 512:(c + 1) * 512] for t in wb]) for c in range(C)],
                   before + [("lo", "wb", c) for c in range(C)], ("RA", k), last=False)
            q = k % 2
            lg, so, cu, t8, su, w8, oh = (sp[:, q, 8 * m:8 * m + 8] for m in range(7))
            kz, ts, rk, tau = (sp[:, q, 56 + m:57 + m] for m in range(4))
            name = ("sp", k)

            def chain(m, fn, *more):
                op("dve", fn, [*more, *([name + (m - 1,)] if m else [])], name + (m,))

            chain(0, lambda e: e.tensor_tensor(out=lg, in0=ra[:, 0:8], in1=br[:, :], op=ALU.add), ("R", k), "bias")
            chain(1, lambda e: e.max(so, lg))
            chain(2, lambda e: e.tensor_tensor_scan(cu, ones8[:, :], so, 0.0, ALU.mult, ALU.add), "ones8")
            chain(3, lambda e: e.tensor_tensor(out=t8, in0=so, in1=kk[:, :], op=ALU.mult), "kk")
            chain(4, lambda e: e.scalar_tensor_tensor(out=su, in0=t8, scalar=1.0, in1=cu, op0=ALU.add,
                                                      op1=ALU.is_gt, accum_out=kz))
            chain(5, lambda e: e.reciprocal(rk, kz))
            chain(6, lambda e: e.scalar_tensor_tensor(out=oh, in0=kk[:, :], scalar=kz, in1=cu, op0=ALU.is_equal,
                                                      op1=ALU.mult, accum_out=ts))
            chain(7, lambda e: e.tensor_scalar(tau, ts, -1.0, rk, ALU.add, ALU.mult))
            chain(8, lambda e: e.tensor_scalar(w8, lg, tau, 0.0, ALU.subtract, ALU.max))
            chain(9, lambda e: e.tensor_tensor(
                out=hw[:, q, :].rearrange("p (a r) -> p a r", a=8),
                in0=ra[:, 8:136].rearrange("p (a r) -> p a r", a=8),
                in1=w8.rearrange("p (a r) -> p a r", r=1).to_broadcast([128, 8, 16]), op=ALU.mult))
            give(n, name + (9,))

        def ffn_experts(k):
            q = k % 2
            out, n, before = take("T")
            op("pe", lambda e: e.transpose(out[:, 0:128], hw[:, q, :], ident[:, :]), before + [("sp", k, 9)], ("ht", k))
            split(out[:, 0:128], hwT[0][:, q, :], hwT[1][:, q, :], ("hwT", k),
                  [("ht", k)] + ([("F", k - 2)] if k >= 2 else []))
            give(n, ("lo", "hwT", k))

        def ffn_sum(k):
            q = k % 2
            base, m, _ = ffn_bank[k]
            passes(base[:, :], [([t[:, q, :] for t in hwT], lb)], [("lo", "hwT", k), ("lo", "lb")], ("F", k), first=False)
            op("dve", lambda e: e.tensor_tensor(out=y[:, k, :], in0=base[:, :], in1=y[:, k, :], op=ALU.add),
               [("F", k), ("zb", k)], ("y2", k))
            give(m, ("y2", k))
            norm_of(y[:, k, :], y[:, k, :], k, ("ln2", k), [("y2", k)])
            op("sp", lambda e: e.dma_start(out_d[k * 128:(k + 1) * 128, :], y[:, k, :]), [("ln2", k)],
               ("out", k), dma="out")

        op("pool", lambda e: e.memset(mask[:, :], 0.0), mark="mask0")
        op("pool", lambda e: e.memset(ident[:, :], 0.0), mark="ident0")
        op("pool", lambda e: e.affine_select(out=mask[:, 384:512], in_=mask[:, 384:512], compare_op=ALU.is_ge,
                                             fill=-BIG, base=0, pattern=[[-1, 128]], channel_multiplier=1),
           ["mask0"], "mask")
        op("pool", lambda e: e.affine_select(out=ident[:, :], in_=ident[:, :], compare_op=ALU.not_equal, fill=1.0,
                                             base=0, pattern=[[-1, 128]], channel_multiplier=1), ["ident0"], "ident")
        op("pool", lambda e: e.memset(mhalf[:, :], -0.5), mark="mhalf")
        op("pool", lambda e: e.memset(ones8[:, :], 1.0), mark="ones8")
        for m in range(8):
            op("pool", lambda e, m=m: e.memset(kk[:, m:m + 1], float(m + 1)), mark="kk")

        load_wk(0, "dve")
        for c in range(C):
            load_x(0, c, "dve")
        for h in range(HG):
            load_wq(0, h, "pool" if h % 2 else "dve")
        for k in range(2):
            load_wv(0, k, "dve" if k else "pool")
        project_k(0)
        for h in range(HG):
            project_q(0, h)
        for c in range(C):
            load_x(1, c, "pool")
        op("sp", lambda e: e.dma_start(y[:, :, :], x_d.rearrange("(k p) n -> p k n", p=128)), mark="x", dma="x")
        for h in range(HG):
            load_wo(0, h)
        op("sp", lambda e: e.dma_start(bb[:, :], bb_d.rearrange("(a n) -> a n", a=1).to_broadcast([128, 512])),
           mark="bias", dma="b")
        op("sp", lambda e: e.dma_start(br[:, :], br_d.rearrange("(a n) -> a n", a=1).to_broadcast([128, 8])),
           mark="bias", dma="b")
        scores(0)
        for tt in range(4):
            project_v(0, tt)
            if tt == 1:
                normalise(0)

        def loads(u, i):
            g, b = divmod(u, B)
            if b == 0 and i == 0 and g:
                load_wo(g, 2)
                load_wo(g, 3)
            if g == G - 1:
                return
            if b == 0:
                if i in (1, 2):
                    load_wo(g + 1, i - 1)
                if g % 2 == 1 and i >= 2:
                    load_wv((g + 1) // 2, i - 2)
            else:
                if i == 0:
                    load_wk(g + 1)
                    load_wq(g + 1, 0)
                if i == 1:
                    load_wq(g + 1, 1)
                    load_wq(g + 1, 2)
                if i == 2:
                    load_wq(g + 1, 3)

        def v_tile(u, i):
            g, b = divmod(u, B)
            if g % 2 == 0 and b == 0:
                return g // 2, 4 + i
            if g % 2 == 1 and b == 1 and g + 1 < G:
                return (g + 1) // 2, i

        def load_ffn():
            done = [("Q", NU - 1, HG - 1), ("Vp", 3, 7)]
            for c in range(C):
                piece(("wb", c), wb_v[:, c, :], [t[:, c * 512:(c + 1) * 512] for t in wb], after=done)
            piece(("wra",), wra_v, [t for t in wra], cols=544, shape=C, after=done)
            piece(("lb",), lb_d, [t for t in lb], after=done)

        for t in range(NT):
            u, i = divmod(t, NI)
            if i == NI - 1 and u + 1 < NU:
                project_k(u + 1)
                for h in range(HG):
                    project_q(u + 1, h)
            if i == NI - 1 and u + 1 < NU and t:
                for h in range(HG):
                    out_proj(t - 1, h)
                wos = []
            else:
                wos = list(range(HG)) if t else []
            if t + 1 < NT:
                scores(t + 1)
            tv = v_tile(u, i)
            turn(t, 0)
            if i:
                turn(t, 1)
            if t + 1 < NT:
                normalise(t + 1)
            if tv:
                project_v(*tv)
            for j in range(2, i + 3):
                if wos:
                    out_proj(t - 1, wos.pop(0))
                if j <= i:
                    turn(t, j)
                if j - 2 == i:
                    while wos:
                        out_proj(t - 1, wos.pop(0))
                weigh(t, j - 2)
            loads(u, i)
            if u == NU - 2 and i == NI - 1:
                load_ffn()
            if u == NU - 1:
                if i >= 1:
                    ffn_norm(i - 1)
                    ffn_turn(i - 1)
                    ffn_products(i - 1)
                if i >= 2:
                    ffn_experts(i - 2)
                    ffn_sum(i - 2)
        for h in range(HG):
            out_proj(NT - 1, h)
        ffn_norm(3)
        for k in range(3, 9):
            if k < 8:
                ffn_turn(k)
                ffn_products(k)
            if k + 1 < 8:
                ffn_norm(k + 1)
            ffn_experts(k - 1)
            ffn_sum(k - 1)

        block = ctx.enter_context(nc.Block())

        @block.sync
        def _(eng):
            play("sp", eng)
            eng.wait_ge(s_out, 16 * 8)

        @block.gpsimd
        def _(eng):
            play("pool", eng)

        @block.scalar
        def _(eng):
            play("act", eng)

        @block.vector
        def _(eng):
            play("dve", eng)

        @block.tensor
        def _(eng):
            play("pe", eng)


def kernel(L0_attn_hidden_states, L0_attn_Wq, L0_attn_Wk, L0_attn_Wv, L0_attn_Wo, L0_ffn_W_base, L0_ffn_b_base,
           L0_ffn_W_router, L0_ffn_b_router, L0_ffn_lora_A, L0_ffn_lora_B):
    import concourse.bacc as bacc
    from concourse.bass_utils import run_bass_kernel_spmd

    x = np.asarray(L0_attn_hidden_states).reshape(1024, 512)
    router = np.asarray(L0_ffn_W_router).T
    lora_a = np.asarray(L0_ffn_lora_A).transpose(1, 0, 2).reshape(512, 128)
    arrays = {
        "xT": x.T, "x": x,
        "wq": L0_attn_Wq, "wk": L0_attn_Wk, "wv": L0_attn_Wv, "wo": L0_attn_Wo,
        "wb": np.asarray(L0_ffn_W_base).T, "wra": np.concatenate([router, lora_a], axis=1),
        "lb": np.asarray(L0_ffn_lora_B).reshape(128, 512),
        "bb": L0_ffn_b_base, "br": L0_ffn_b_router,
    }
    arrays = {n: np.ascontiguousarray(a) for n, a in arrays.items()}
    nc = bacc.Bacc("TRN2", target_bir_lowering=False, num_devices=1)
    args = [nc.dram_tensor(f"in_{n}", a.shape, mybir.dt.from_np(a.dtype), kind="ExternalInput").ap()
            for n, a in arrays.items()]
    args.append(nc.dram_tensor("out", (1024, 512), mybir.dt.float32, kind="ExternalOutput").ap())
    post_ln_block(nc, *args)
    r = run_bass_kernel_spmd(nc, [{f"in_{n}": a for n, a in arrays.items()}], core_ids=[0])
    return r.results[0]["out"].reshape(2, 512, 512)
```

```python
import numpy as np
import concourse.bass as bass
from concourse import mybir
from contextlib import ExitStack


def post_ln_block(nc, xT_d, x_d, wq_d, wk_d, wv_d, wo_d, wb_d, wra_d, lb_d, bb_d, br_d, out_d):
    f32, f32r = mybir.dt.float32, mybir.dt.float32r
    ALU, ACT = mybir.AluOpType, mybir.ActivationFunctionType

    G, B, NI, HG, C = 8, 2, 4, 4, 4
    NU, NT = G * B, G * B * NI
    SCALE = 128.0 ** -0.5
    EPS = 1e-5
    NRAW, NWO, NV, NPT = 6, 6, 12, 4
    BIG = 3.0e38

    ctx = ExitStack()
    with ctx:
        def sb(name, shape, dt=f32):
            return ctx.enter_context(nc.sbuf_tensor(name, shape, dt))

        def sem(name):
            return ctx.enter_context(nc.semaphore(name))

        raw = sb("raw", [128, NRAW, 544])
        xT = [sb("xT_hi", [128, C, 1024], f32r), sb("xT_lo", [128, C, 1024], f32r)]
        wq = [sb("wq_hi", [128, HG, 512], f32r), sb("wq_lo", [128, HG, 512], f32r)]
        wk = [sb("wk_hi", [128, 512], f32r), sb("wk_lo", [128, 512], f32r)]
        wv = [sb("wv_hi", [128, 1024], f32r), sb("wv_lo", [128, 1024], f32r)]
        wo = [sb("wo_hi", [128, NWO, 512], f32r), sb("wo_lo", [128, NWO, 512], f32r)]
        kT = [sb("kT_hi", [128, 512], f32r), sb("kT_lo", [128, 512], f32r)]
        qT = [sb("qT_hi", [128, HG, 512], f32r), sb("qT_lo", [128, HG, 512], f32r)]
        v = [sb("v_hi", [128, NV, 256], f32r), sb("v_lo", [128, NV, 256], f32r)]
        pr = sb("pr", [128, 8, 512])
        pT = [sb("pT_hi", [128, NPT, 512], f32r), sb("pT_lo", [128, NPT, 512], f32r)]
        oT = [sb("oT_hi", [128, 2, 512], f32r), sb("oT_lo", [128, 2, 512], f32r)]
        y = sb("y", [128, 8, 512])
        mask = sb("mask", [128, 512])
        ident = sb("ident", [128, 128])
        mx = sb("mx", [128, 8])
        rs = sb("rs", [128, 8])
        ri = sb("ri", [128, 8])
        bb = sb("bb", [128, 512])
        br = sb("br", [128, 8])
        kk = sb("kk", [128, 8])
        ones8 = sb("ones8", [128, 8])
        mhalf = sb("mhalf", [128, 1])
        st = sb("st", [128, 4, 6])
        mv = sb("mv", [128, 4, 2])
        vs = sb("vs", [128, 4])
        rstd = sb("rstd", [128, 4])
        sp = sb("sp", [128, 2, 64])
        hw = sb("hw", [128, 2, 128])
        hwT = [sb("hwT_hi", [128, 2, 128], f32r), sb("hwT_lo", [128, 2, 128], f32r)]
        zT = [wq[0], wq[1]]
        wb = [x[:, 0:2, :].rearrange("p a n -> p (a n)") for x in xT]
        wra = [x[:, 2, 0:544] for x in xT]
        lb = [x[:, 3, 0:512] for x in xT]

        bank = [ctx.enter_context(nc.psum_tensor(f"bank{n}", [128, 512], f32)) for n in range(8)]
        S_BANKS, T_BANKS, A_BANKS = bank[0:3], bank[3:5], bank[5:8]

        sems = {e: sem(f"s_{e}") for e in ("pe", "act", "dve", "pool")}
        s_raw = [sem(f"s_raw{n}") for n in range(NRAW)]
        s_x, s_b, s_out = sem("s_x"), sem("s_b"), sem("s_out")
        sems.update({f"raw{n}": s for n, s in enumerate(s_raw)})
        sems.update(x=s_x, b=s_b, out=s_out)

        queue = {e: [] for e in ("pe", "act", "dve", "pool", "sp")}
        count = {}
        at = {}

        def op(engine, fn, waits=(), mark=None, dma=None):
            name = dma or engine
            found = [at[w] for w in waits]
            by = 0
            if mark is not None:
                by = 16 if dma else 1
                count[name] = count.get(name, 0) + by
                at[mark] = (name, count[name])
            queue[engine].append((found, fn, name, by))

        def play(engine, eng):
            seen = {}
            for found, fn, name, by in queue[engine]:
                for s, n in found:
                    if seen.get(s, 0) < n:
                        eng.wait_ge(sems[s], n)
                        seen[s] = n
                ins = fn(eng)
                if by:
                    ins.then_inc(sems[name], by)

        def raw_of(t):
            return t.bitcast(f32)

        free = {"S": [(x, []) for x in S_BANKS], "T": [(x, []) for x in T_BANKS], "A": [(x, []) for x in A_BANKS]}

        def take(kind):
            out, before = free[kind].pop(0)
            return out, (kind, out), before

        def give(place, mark):
            free[place[0]].append((place[1], [mark]))

        def passes(out, pairs, waits, mark, first=True, last=True):
            todo = [(a[i], b[j]) for a, b in pairs for i, j in ((0, 0), (0, 1), (1, 0))]
            for n, (a, b) in enumerate(todo):
                op("pe", lambda e, a=a, b=b, s=first and n == 0, t=last and n == len(todo) - 1:
                   e.matmul(out, a, b, start=s, stop=t),
                   waits if n == 0 else (), mark if n == len(todo) - 1 else None)

        def split(src, hi, lo, name, waits, hi_engine="act", lo_engine="dve"):
            if hi_engine == "act":
                op("act", lambda e: e.activation(hi, src, ACT.Copy), waits, ("hi",) + name)
            else:
                op(hi_engine, lambda e: e.tensor_copy(hi, src), waits, ("hi",) + name)
            op(lo_engine, lambda e: e.tensor_tensor(out=lo, in0=src, in1=raw_of(hi), op=ALU.subtract),
               [("hi",) + name], ("lo",) + name)

        pieces = [0]

        def piece(name, src, dst, cols=512, shape=None, after=(), lo_engine="pool", hi_engine="act"):
            n = pieces[0]
            pieces[0] += 1
            slot = n % NRAW
            r = raw[:, slot, 0:cols]
            rv = r.rearrange("p (c n) -> p c n", c=shape) if shape else r
            op("sp", lambda e: e.dma_start(rv, src), [("piece", n - NRAW)] if n >= NRAW else [],
               ("raw", n), dma=f"raw{slot}")
            split(r if cols == dst[0].shape[-1] else rv, dst[0], dst[1], name, [("raw", n), *after],
                  hi_engine, lo_engine)
            at["piece", n] = at[("lo",) + name]

        wq_v = wq_d.rearrange("(c p) n -> p c n", p=128)
        wk_v = wk_d.rearrange("(c p) n -> p c n", p=128)
        wv_v = wv_d.rearrange("(c p) n -> p c n", p=128)
        wo_v = wo_d.rearrange("(h p) n -> p h n", p=128)
        xT_v = xT_d.rearrange("(c p) t -> p c t", p=128)
        wb_v = wb_d.rearrange("(c p) n -> p c n", p=128)
        wra_v = wra_d.rearrange("(c p) n -> p c n", p=128)

        def load_x(b, c, lo_engine):
            piece(("x", b, c), xT_v[:, c, b * 512:(b + 1) * 512],
                  [t[:, c, b * 512:(b + 1) * 512] for t in xT], lo_engine=lo_engine)

        def load_wk(g, lo_engine="pool"):
            piece(("wk", g), wk_v[:, :, g * 128:(g + 1) * 128], [t[:, :] for t in wk], shape=C,
                  after=[("K", 2 * g - 1)] if g else [], lo_engine=lo_engine)

        def load_wq(g, h, lo_engine="pool"):
            n = HG * g + h
            piece(("wq", g, h), wq_v[:, :, n * 128:(n + 1) * 128], [t[:, h, :] for t in wq], shape=C,
                  after=[("Q", 2 * g - 1, h)] if g else [], lo_engine=lo_engine)

        def load_wo(g, h, lo_engine="pool"):
            n = HG * g + h
            old = (n - NWO) // HG
            piece(("wo", g, h), wo_v[:, n, :], [t[:, n % NWO, :] for t in wo],
                  after=[("W", 8 * old + 7)] if n >= NWO else [], lo_engine=lo_engine)

        def load_wv(p, k, lo_engine="pool"):
            piece(("wv", p, k), wv_v[:, 2 * k:2 * k + 2, p * 256:(p + 1) * 256],
                  [t[:, k * 512:(k + 1) * 512] for t in wv], shape=2,
                  after=[("Vp", p - 1, 7)] if p else [], lo_engine=lo_engine)

        def x_of(b):
            return [("lo", "x", b, c) for c in range(C)]

        def project_k(u):
            g, b = divmod(u, B)
            out, n, before = take("A")
            passes(out[:, :], [([t[:, c * 128:(c + 1) * 128] for t in wk],
                                [t[:, c, b * 512:(b + 1) * 512] for t in xT]) for c in range(C)],
                   before + [("lo", "wk", g)] + x_of(b), ("K", u))
            split(out[:, :], kT[0][:, :], kT[1][:, :], ("kT", u),
                  [("K", u)] + ([("S", 4 * u - 1, HG - 1)] if u else []))
            give(n, ("lo", "kT", u))

        def project_q(u, h):
            g, b = divmod(u, B)
            out, n, before = take("A")
            passes(out[:, :], [([t[:, h, c * 128:(c + 1) * 128] for t in wq],
                                [t[:, c, b * 512:(b + 1) * 512] for t in xT]) for c in range(C)],
                   before + [("lo", "wq", g, h)] + x_of(b), ("Q", u, h))
            split(out[:, :], qT[0][:, h, :], qT[1][:, h, :], ("qT", u, h),
                  [("Q", u, h)] + ([("S", 4 * u - 1, h)] if u else []))
            give(n, ("lo", "qT", u, h))

        def v_slot(p, tt):
            return (8 * p + tt) % NV

        def project_v(p, tt):
            out, n, before = take("A")
            old = 8 * p + tt - NV
            after = []
            if old >= 0:
                op_, ot = divmod(old, 8)
                after = [("V", 4 * (2 * (2 * op_ + 1) + ot // 4) + 3, 3)]
            passes(out[:, 0:256], [([t[:, c, tt * 128:(tt + 1) * 128] for t in xT],
                                    [t[:, c * 256:(c + 1) * 256] for t in wv]) for c in range(C)],
                   before + [("lo", "wv", p, 0), ("lo", "wv", p, 1)] + x_of(tt // 4), ("Vp", p, tt))
            s = v_slot(p, tt)
            split(out[:, 0:256], v[0][:, s, :], v[1][:, s, :], ("v", p, tt), [("Vp", p, tt)] + after)
            give(n, ("lo", "v", p, tt))

        def score(t, h):
            if t >= NT:
                return
            u, i = divmod(t, NI)
            w = 128 * (i + 1)
            k = 4 * (t % 2) + h
            out, n, before = take("S")
            passes(out[:, 0:w], [([x[:, h, i * 128:(i + 1) * 128] for x in qT], [x[:, 0:w] for x in kT])],
                   before + [("lo", "qT", u, h), ("lo", "kT", u)], ("S", t, h))
            op("dve", lambda e: e.tensor_tensor_reduce(
                out=pr[:, k, 0:w], in0=out[:, 0:w], in1=mask[:, 512 - w:512], scale=-SCALE, scalar=BIG,
                op0=ALU.add, op1=ALU.min, accum_out=mx[:, k:k + 1]),
               [("S", t, h), "mask"] + ([("T", t - 2, (t - 2) % NI)] if t >= 2 else []), ("max", t, h))
            give(n, ("max", t, h))

        def exponent(t, h):
            if t >= NT:
                return
            w = 128 * (t % NI + 1)
            k = 4 * (t % 2) + h
            op("act", lambda e: e.activation(
                pr[:, k, 0:w], pr[:, k, 0:w], ACT.Exp, bias=mx[:, k:k + 1], scale=-1.0,
                accum_out=rs[:, k:k + 1]), [("max", t, h)], ("exp", t, h))

        def normalise(t):
            if t >= NT:
                return
            w = 128 * (t % NI + 1)
            k0 = 4 * (t % 2)
            op("dve", lambda e: e.reciprocal(ri[:, k0:k0 + 4], rs[:, k0:k0 + 4]), [("exp", t, HG - 1)],
               ("ri", t))
            for h in range(HG):
                k = k0 + h
                p = pr[:, k, 0:w]
                if h < 1:
                    op("pool", lambda e, p=p, k=k: e.tensor_tensor(
                        out=p, in0=p, in1=ri[:, k:k + 1].to_broadcast([128, w]), op=ALU.mult),
                       [("ri", t)], ("p", t, h))
                else:
                    op("dve", lambda e, p=p, k=k: e.tensor_scalar(p, p, ri[:, k:k + 1], None, ALU.mult),
                       [("ri", t)], ("p", t, h))

        pt_at, pt_n = {}, [0]

        def turn(t, j):
            out, n, before = take("T")
            for h in range(HG):
                op("pe", lambda e, h=h: e.transpose(out[:, h * 128:(h + 1) * 128],
                                                    pr[:, 4 * (t % 2) + h, j * 128:(j + 1) * 128], ident[:, :]),
                   (before + ["ident"] if h == 0 else []) + [("p", t, h)], ("T", t, j) if h == HG - 1 else None)
            s = pt_n[0]
            pt_n[0] += 1
            pt_at[s] = (t, j)
            split(out[:, :], pT[0][:, s % NPT, :], pT[1][:, s % NPT, :], ("pT", t, j),
                  [("T", t, j)] + ([("V", *pt_at[s - NPT])] if s >= NPT else []))
            pt_at[t, j] = s % NPT
            give(n, ("lo", "pT", t, j))

        pv_bank = {}

        def weigh(t, j):
            u, i = divmod(t, NI)
            g, b = divmod(u, B)
            if j == 0:
                pv_bank[t] = take("A")
            out, n, before = pv_bank[t]
            s, k = v_slot(g // 2, 4 * b + j), pt_at[t, j]
            cols = slice((g % 2) * 128, (g % 2) * 128 + 128)
            passes(out[:, :], [([x[:, s, cols] for x in v], [x[:, k, :] for x in pT])],
                   (before if j == 0 else []) + [("lo", "pT", t, j), ("lo", "v", g // 2, 4 * b + j)],
                   ("V", t, j), j == 0, j == i)
            if j == i:
                split(out[:, :], oT[0][:, t % 2, :], oT[1][:, t % 2, :], ("oT", t),
                      [("V", t, i)] + ([("W", t - 2)] if t >= 2 else []))
                give(n, ("lo", "oT", t))

        wo_bank = {}

        def out_proj(t, h):
            u, i = divmod(t, NI)
            g, b = divmod(u, B)
            if h == 0:
                wo_bank[t] = take("A")
            out, n, before = wo_bank[t]
            s = (HG * g + h) % NWO
            passes(out[:, :], [([x[:, t % 2, h * 128:(h + 1) * 128] for x in oT], [x[:, s, :] for x in wo])],
                   (before if h == 0 else []) + [("lo", "oT", t), ("lo", "wo", g, h)],
                   ("W", t) if h == HG - 1 else None, h == 0, h == HG - 1)
            if h == HG - 1:
                k = 4 * b + i
                op("dve", lambda e: e.tensor_tensor(out=y[:, k, :], in0=out[:, :], in1=y[:, k, :], op=ALU.add),
                   [("W", t), ("y", g - 1, k) if g else "x"], ("y", g, k))
                give(n, ("y", g, k))
                if g == G - 1:
                    ffn_norm(k)

        def norm_of(src, dst, k, name, waits):
            n = name[1] % 2 + (2 if name[0] == "ln2" else 0)
            op("dve", lambda e: e.bn_stats(st[:, n, :], src), waits, name + ("st",))
            op("dve", lambda e: e.bn_aggr(mv[:, n, :], st[:, n, :]), [name + ("st",)], name + ("mv",))
            op("pool", lambda e: e.tensor_scalar(vs[:, n:n + 1], mv[:, n, 1:2], EPS, None, ALU.add),
               [name + ("mv",)], name + ("vs",))
            op("pool", lambda e: e.tensor_tensor(out=rstd[:, n:n + 1], in0=vs[:, n:n + 1], in1=mhalf[:, :],
                                                 op=ALU.pow), [name + ("vs",), "mhalf"], name + ("rstd",))
            op("dve", lambda e: e.tensor_scalar(dst, src, mv[:, n, 0:1], rstd[:, n:n + 1], ALU.subtract, ALU.mult),
               [name + ("rstd",)], name)

        def ffn_norm(k):
            norm_of(y[:, k, :], y[:, k, :], k, ("ln1", k), [("y", G - 1, k)])

        def ffn_turn(k):
            out, n, before = take("T")
            for c in range(C):
                op("pe", lambda e, c=c: e.transpose(out[:, c * 128:(c + 1) * 128], y[:, k, c * 128:(c + 1) * 128],
                                                    ident[:, :]),
                   before + [("ln1", k)] if c == 0 else (), ("zt", k) if c == C - 1 else None)
            after = [("base", k - 2)] if k >= 2 else [("Q", NU - 1, HG - 1)]
            split(out[:, :], zT[0][:, k % 2, :], zT[1][:, k % 2, :], ("zT", k), [("zt", k)] + after)
            give(n, ("lo", "zT", k))
            op("pool", lambda e: e.tensor_tensor(out=y[:, k, :], in0=y[:, k, :], in1=bb[:, :], op=ALU.add),
               [("zt", k), "bias"], ("zb", k))

        ffn_bank = {}

        def ffn_lhs(k):
            return [[t[:, k % 2, c * 128:(c + 1) * 128] for t in zT] for c in range(C)]

        def ffn_base(k):
            ffn_bank[k] = take("A")
            base, _, before = ffn_bank[k]
            passes(base[:, :], [(a, [t[:, c * 512:(c + 1) * 512] for t in wb]) for c, a in enumerate(ffn_lhs(k))],
                   before + [("lo", "zT", k)] + [("lo", "wb", c) for c in range(C)], ("base", k), last=False)

        def ffn_route(k):
            ra, n, before = take("S")
            passes(ra[:, 0:136], [(a, [t[:, c * 136:(c + 1) * 136] for t in wra]) for c, a in enumerate(ffn_lhs(k))],
                   before + [("lo", "zT", k), ("lo", "wra")], ("R", k))
            q = k % 2
            lg, so, cu, t8, su, w8, oh = (sp[:, q, 8 * m:8 * m + 8] for m in range(7))
            kz, ts, rk, tau = (sp[:, q, 56 + m:57 + m] for m in range(4))
            name = ("sp", k)

            def chain(m, fn, *more):
                op("dve", fn, [*more, *([name + (m - 1,)] if m else [])], name + (m,))

            chain(0, lambda e: e.tensor_tensor(out=lg, in0=ra[:, 0:8], in1=br[:, :], op=ALU.add), ("R", k), "bias")
            chain(1, lambda e: e.max(so, lg))
            chain(2, lambda e: e.tensor_tensor_scan(cu, ones8[:, :], so, 0.0, ALU.mult, ALU.add), "ones8")
            chain(3, lambda e: e.tensor_tensor(out=t8, in0=so, in1=kk[:, :], op=ALU.mult), "kk")
            chain(4, lambda e: e.scalar_tensor_tensor(out=su, in0=t8, scalar=1.0, in1=cu, op0=ALU.add,
                                                      op1=ALU.is_gt, accum_out=kz))
            chain(5, lambda e: e.reciprocal(rk, kz))
            chain(6, lambda e: e.scalar_tensor_tensor(out=oh, in0=kk[:, :], scalar=kz, in1=cu, op0=ALU.is_equal,
                                                      op1=ALU.mult, accum_out=ts))
            chain(7, lambda e: e.tensor_scalar(tau, ts, -1.0, rk, ALU.add, ALU.mult))
            chain(8, lambda e: e.tensor_scalar(w8, lg, tau, 0.0, ALU.subtract, ALU.max))
            chain(9, lambda e: e.tensor_tensor(
                out=hw[:, q, :].rearrange("p (a r) -> p a r", a=8),
                in0=ra[:, 8:136].rearrange("p (a r) -> p a r", a=8),
                in1=w8.rearrange("p (a r) -> p a r", r=1).to_broadcast([128, 8, 16]), op=ALU.mult))
            give(n, name + (9,))

        def ffn_experts(k):
            q = k % 2
            out, n, before = take("T")
            op("pe", lambda e: e.transpose(out[:, 0:128], hw[:, q, :], ident[:, :]), before + [("sp", k, 9)], ("ht", k))
            split(out[:, 0:128], hwT[0][:, q, :], hwT[1][:, q, :], ("hwT", k),
                  [("ht", k)] + ([("F", k - 2)] if k >= 2 else []))
            give(n, ("lo", "hwT", k))

        def ffn_sum(k):
            q = k % 2
            base, m, _ = ffn_bank[k]
            passes(base[:, :], [([t[:, q, :] for t in hwT], lb)], [("lo", "hwT", k), ("lo", "lb")], ("F", k), first=False)
            op("dve", lambda e: e.tensor_tensor(out=y[:, k, :], in0=base[:, :], in1=y[:, k, :], op=ALU.add),
               [("F", k), ("zb", k)], ("y2", k))
            give(m, ("y2", k))
            norm_of(y[:, k, :], y[:, k, :], k, ("ln2", k), [("y2", k)])
            op("sp", lambda e: e.dma_start(out_d[k * 128:(k + 1) * 128, :], y[:, k, :]), [("ln2", k)],
               ("out", k), dma="out")

        op("pool", lambda e: e.memset(mask[:, :], 0.0), mark="mask0")
        op("pool", lambda e: e.memset(ident[:, :], 0.0), mark="ident0")
        op("pool", lambda e: e.affine_select(out=mask[:, 384:512], in_=mask[:, 384:512], compare_op=ALU.is_ge,
                                             fill=-BIG, base=0, pattern=[[-1, 128]], channel_multiplier=1),
           ["mask0"], "mask")
        op("pool", lambda e: e.affine_select(out=ident[:, :], in_=ident[:, :], compare_op=ALU.not_equal, fill=1.0,
                                             base=0, pattern=[[-1, 128]], channel_multiplier=1), ["ident0"], "ident")
        op("pool", lambda e: e.memset(mhalf[:, :], -0.5), mark="mhalf")
        op("pool", lambda e: e.memset(ones8[:, :], 1.0), mark="ones8")
        for m in range(8):
            op("pool", lambda e, m=m: e.memset(kk[:, m:m + 1], float(m + 1)), mark="kk")

        load_wk(0, "dve")
        for c in range(C):
            load_x(0, c, "dve")
        for h in range(HG):
            load_wq(0, h, "pool" if h % 2 else "dve")
        for k in range(2):
            load_wv(0, k, "dve" if k else "pool")
        project_k(0)
        for h in range(HG):
            project_q(0, h)
        for c in range(C):
            load_x(1, c, "pool")
        op("sp", lambda e: e.dma_start(y[:, :, :], x_d.rearrange("(k p) n -> p k n", p=128)), mark="x", dma="x")
        for h in range(HG):
            load_wo(0, h)
        op("sp", lambda e: e.dma_start(bb[:, :], bb_d.rearrange("(a n) -> a n", a=1).to_broadcast([128, 512])),
           mark="bias", dma="b")
        op("sp", lambda e: e.dma_start(br[:, :], br_d.rearrange("(a n) -> a n", a=1).to_broadcast([128, 8])),
           mark="bias", dma="b")
        for h in range(HG):
            score(0, h)
            exponent(0, h)
        for tt in range(4):
            project_v(0, tt)
            if tt == 1:
                normalise(0)

        def loads(u, i):
            g, b = divmod(u, B)
            if b == 0 and i == 0 and g:
                load_wo(g, 2)
                load_wo(g, 3)
            if g == G - 1:
                return
            if b == 0:
                if i in (1, 2):
                    load_wo(g + 1, i - 1)
                if g % 2 == 1 and i >= 2:
                    load_wv((g + 1) // 2, i - 2)
            else:
                if i == 0:
                    load_wk(g + 1)
                    load_wq(g + 1, 0)
                if i == 1:
                    load_wq(g + 1, 1)
                    load_wq(g + 1, 2)
                if i == 2:
                    load_wq(g + 1, 3)

        def v_tile(u, i):
            g, b = divmod(u, B)
            if g % 2 == 0 and b == 0:
                return g // 2, 4 + i
            if g % 2 == 1 and b == 1 and g + 1 < G:
                return (g + 1) // 2, i

        def load_ffn():
            done = [("Q", NU - 1, HG - 1), ("Vp", 3, 7)]
            for c in range(C):
                piece(("wb", c), wb_v[:, c, :], [t[:, c * 512:(c + 1) * 512] for t in wb], after=done)
            piece(("wra",), wra_v, [t for t in wra], cols=544, shape=C, after=done)
            piece(("lb",), lb_d, [t for t in lb], after=done)

        second = [("turn", 0), ("route", 0)]
        for k in range(8):
            second += [("turn", k + 1), ("base", k), ("experts", k), ("route", k + 1), ("sum", k)]
        second = [x for x in second if x[1] < 8]
        work = {"turn": ffn_turn, "base": ffn_base, "experts": ffn_experts, "route": ffn_route, "sum": ffn_sum}

        def second_half(n):
            for _ in range(min(n, len(second))):
                what, k = second.pop(0)
                work[what](k)

        for t in range(NT):
            u, i = divmod(t, NI)
            burst = i == NI - 1 and u + 1 < NU
            late = u == NU - 1
            tv = v_tile(u, i)
            wos = list(range(HG)) if t else []

            def filler():
                if wos:
                    out_proj(t - 1, wos.pop(0))
                if late:
                    second_half(1)

            if burst:
                project_k(u + 1)
            turn(t, 0)
            if burst:
                turn(t, 1)
                project_q(u + 1, 0)
                weigh(t, 0)
                turn(t, 2)
                weigh(t, 1)
                project_q(u + 1, 1)
                turn(t, 3)
                weigh(t, 2)
                project_q(u + 1, 2)
                weigh(t, 3)
                project_q(u + 1, 3)
                if u == NU - 2:
                    load_ffn()
                if tv:
                    project_v(*tv)
                filler()
                filler()
                for h in range(HG):
                    score(t + 1, h)
                    exponent(t + 1, h)
                normalise(t + 1)
                filler()
                filler()
            else:
                score(t + 1, 0)
                if i >= 1:
                    turn(t, 1)
                exponent(t + 1, 0)
                score(t + 1, 1)
                filler()
                if i >= 2:
                    turn(t, 2)
                exponent(t + 1, 1)
                score(t + 1, 2)
                if i >= 3:
                    turn(t, 3)
                exponent(t + 1, 2)
                score(t + 1, 3)
                exponent(t + 1, 3)
                normalise(t + 1)
                for j in range(i + 1):
                    if j:
                        filler()
                    weigh(t, j)
                if tv:
                    project_v(*tv)
                while wos:
                    filler()
            loads(u, i)
        second_half(2)
        for h in range(HG):
            out_proj(NT - 1, h)
        second_half(len(second))

        block = ctx.enter_context(nc.Block())

        @block.sync
        def _(eng):
            play("sp", eng)
            eng.wait_ge(s_out, 16 * 8)

        @block.gpsimd
        def _(eng):
            play("pool", eng)

        @block.scalar
        def _(eng):
            play("act", eng)

        @block.vector
        def _(eng):
            play("dve", eng)

        @block.tensor
        def _(eng):
            play("pe", eng)


def kernel(L0_attn_hidden_states, L0_attn_Wq, L0_attn_Wk, L0_attn_Wv, L0_attn_Wo, L0_ffn_W_base, L0_ffn_b_base,
           L0_ffn_W_router, L0_ffn_b_router, L0_ffn_lora_A, L0_ffn_lora_B):
    import concourse.bacc as bacc
    from concourse.bass_utils import run_bass_kernel_spmd

    x = np.asarray(L0_attn_hidden_states).reshape(1024, 512)
    router = np.asarray(L0_ffn_W_router).T
    lora_a = np.asarray(L0_ffn_lora_A).transpose(1, 0, 2).reshape(512, 128)
    arrays = {
        "xT": x.T, "x": x,
        "wq": L0_attn_Wq, "wk": L0_attn_Wk, "wv": L0_attn_Wv, "wo": L0_attn_Wo,
        "wb": np.asarray(L0_ffn_W_base).T, "wra": np.concatenate([router, lora_a], axis=1),
        "lb": np.asarray(L0_ffn_lora_B).reshape(128, 512),
        "bb": L0_ffn_b_base, "br": L0_ffn_b_router,
    }
    arrays = {n: np.ascontiguousarray(a) for n, a in arrays.items()}
    nc = bacc.Bacc("TRN2", target_bir_lowering=False, num_devices=1)
    args = [nc.dram_tensor(f"in_{n}", a.shape, mybir.dt.from_np(a.dtype), kind="ExternalInput").ap()
            for n, a in arrays.items()]
    args.append(nc.dram_tensor("out", (1024, 512), mybir.dt.float32, kind="ExternalOutput").ap())
    post_ln_block(nc, *args)
    r = run_bass_kernel_spmd(nc, [{f"in_{n}": a for n, a in arrays.items()}], core_ids=[0])
    return r.results[0]["out"].reshape(2, 512, 512)
```

```python
import numpy as np
import concourse.bass as bass
from concourse import mybir
from contextlib import ExitStack


def post_ln_block(nc, xT_d, x_d, wq_d, wk_d, wv_d, wo_d, wb_d, wra_d, lb_d, bb_d, br_d, out_d):
    f32, f32r = mybir.dt.float32, mybir.dt.float32r
    ALU, ACT = mybir.AluOpType, mybir.ActivationFunctionType

    G, B, NI, HG, C = 8, 2, 4, 4, 4
    NU, NT = G * B, G * B * NI
    SCALE = 128.0 ** -0.5
    EPS = 1e-5
    NRAW, NWO, NV, NPT = 6, 6, 12, 4
    BIG = 3.0e38

    ctx = ExitStack()
    with ctx:
        def sb(name, shape, dt=f32):
            return ctx.enter_context(nc.sbuf_tensor(name, shape, dt))

        def sem(name):
            return ctx.enter_context(nc.semaphore(name))

        raw = sb("raw", [128, NRAW, 544])
        xT = [sb("xT_hi", [128, C, 1024], f32r), sb("xT_lo", [128, C, 1024], f32r)]
        wq = [sb("wq_hi", [128, HG, 512], f32r), sb("wq_lo", [128, HG, 512], f32r)]
        wk = [sb("wk_hi", [128, 512], f32r), sb("wk_lo", [128, 512], f32r)]
        wv = [sb("wv_hi", [128, 1024], f32r), sb("wv_lo", [128, 1024], f32r)]
        wo = [sb("wo_hi", [128, NWO, 512], f32r), sb("wo_lo", [128, NWO, 512], f32r)]
        kTs = sb("kT", [128, 2, 512], f32r)
        kT = [kTs[:, 0, :], kTs[:, 1, :]]
        qT = [sb("qT_hi", [128, HG, 512], f32r), sb("qT_lo", [128, HG, 512], f32r)]
        vs_ = sb("v", [128, 2, NV, 256], f32r)
        v = [vs_[:, 0, :, :], vs_[:, 1, :, :]]
        pr = sb("pr", [128, 8, 512])
        pT = [sb("pT_hi", [128, NPT, 512], f32r), sb("pT_lo", [128, NPT, 512], f32r)]
        oT = [sb("oT_hi", [128, 2, 512], f32r), sb("oT_lo", [128, 2, 512], f32r)]
        y = sb("y", [128, 8, 512])
        mask = sb("mask", [128, 512])
        ident = sb("ident", [128, 128])
        mx = sb("mx", [128, 8])
        rs = sb("rs", [128, 8])
        ri = sb("ri", [128, 8])
        bb = sb("bb", [128, 512])
        br = sb("br", [128, 8])
        ik = sb("ik", [128, 8])
        ones8 = sb("ones8", [128, 8])
        mhalf = sb("mhalf", [128, 1])
        st = sb("st", [128, 8, 6])
        mv = sb("mv", [128, 8, 2])
        vs = sb("vs", [128, 8])
        rstd = sb("rstd", [128, 8])
        nmr = sb("nmr", [128, 4])
        sp = sb("sp", [128, 2, 64])
        hw = sb("hw", [128, 2, 128])
        rl = sb("rl", [128, 2, 136])
        hwT = [sb("hwT_hi", [128, 2, 128], f32r), sb("hwT_lo", [128, 2, 128], f32r)]
        zT = [wq[0], wq[1]]
        wb = [[x[:, c * 512:(c + 1) * 512] for x in wv] for c in range(2)]
        wb += [[x[:, s, :] for x in wo] for s in (2, 3)]
        wras = vs_[:, :, 8:11, :].rearrange("p s a n -> p s (a n)")[:, :, 0:544]
        wra = [wras[:, 0, :], wras[:, 1, :]]
        lb = [x[:, :] for x in wk]

        bank = [ctx.enter_context(nc.psum_tensor(f"bank{n}", [128, 512], f32)) for n in range(8)]
        S_BANKS, T_BANKS, A_BANKS = bank[0:3], bank[3:5], bank[5:8]

        sems = {e: sem(f"s_{e}") for e in ("pe", "act", "dve", "pool")}
        s_raw = [sem(f"s_raw{n}") for n in range(NRAW)]
        s_x, s_b, s_out = sem("s_x"), sem("s_b"), sem("s_out")
        sems.update({f"raw{n}": s for n, s in enumerate(s_raw)})
        sems.update(x=s_x, b=s_b, out=s_out)

        queue = {e: [] for e in ("pe", "act", "dve", "pool", "sp")}
        count = {}
        at = {}

        def op(engine, fn, waits=(), mark=None, dma=None):
            name = dma or engine
            found = [at[w] for w in waits]
            by = 0
            if mark is not None:
                by = 16 if dma else 1
                count[name] = count.get(name, 0) + by
                at[mark] = (name, count[name])
            queue[engine].append((found, fn, name, by))

        def play(engine, eng):
            seen = {}
            for found, fn, name, by in queue[engine]:
                for s, n in found:
                    if seen.get(s, 0) < n:
                        eng.wait_ge(sems[s], n)
                        seen[s] = n
                ins = fn(eng)
                if by:
                    ins.then_inc(sems[name], by)

        def raw_of(t):
            return t.bitcast(f32)

        free = {"S": [(x, []) for x in S_BANKS], "T": [(x, []) for x in T_BANKS], "A": [(x, []) for x in A_BANKS]}

        def take(kind):
            out, before = free[kind].pop(0)
            return out, (kind, out), before

        def give(place, mark):
            free[place[0]].append((place[1], [mark]))

        def passes(out, pairs, waits, mark, first=True, last=True, each=()):
            todo = [(a[i], b[j], each[c:c + 1] if (i, j) == (0, 0) else ())
                    for c, (a, b) in enumerate(pairs) for i, j in ((0, 0), (0, 1), (1, 0))]
            products(out, todo, waits, mark, first, last)

        def products(out, todo, waits, mark, first=True, last=True):
            for n, (a, b, more) in enumerate(todo):
                op("pe", lambda e, a=a, b=b, s=first and n == 0, t=last and n == len(todo) - 1:
                   e.matmul(out, a, b, start=s, stop=t),
                   [*(waits if n == 0 else ()), *more], mark if n == len(todo) - 1 else None)

        def split(src, hi, lo, name, waits, hi_engine="act", lo_engine="dve"):
            if hi_engine == "act":
                op("act", lambda e: e.activation(hi, src, ACT.Copy), waits, ("hi",) + name)
            else:
                op(hi_engine, lambda e: e.tensor_copy(hi, src), waits, ("hi",) + name)
            op(lo_engine, lambda e: e.tensor_tensor(out=lo, in0=src, in1=raw_of(hi), op=ALU.subtract),
               [("hi",) + name], ("lo",) + name)

        pieces = [0]

        def piece(name, src, dst, cols=512, shape=None, after=(), lo_engine="pool", hi_engine="act"):
            n = pieces[0]
            pieces[0] += 1
            slot = n % NRAW
            r = raw[:, slot, 0:cols]
            rv = r.rearrange("p (c n) -> p c n", c=shape) if shape else r
            op("sp", lambda e: e.dma_start(rv, src), [("piece", n - NRAW)] if n >= NRAW else [],
               ("raw", n), dma=f"raw{slot}")
            split(r if cols == dst[0].shape[-1] else rv, dst[0], dst[1], name, [("raw", n), *after],
                  hi_engine, lo_engine)
            at["piece", n] = at[("lo",) + name]

        wq_v = wq_d.rearrange("(c p) n -> p c n", p=128)
        wk_v = wk_d.rearrange("(c p) n -> p c n", p=128)
        wv_v = wv_d.rearrange("(c p) n -> p c n", p=128)
        wo_v = wo_d.rearrange("(h p) n -> p h n", p=128)
        xT_v = xT_d.rearrange("(c p) t -> p c t", p=128)
        wb_v = wb_d.rearrange("(c p) n -> p c n", p=128)
        wra_v = wra_d.rearrange("(c p) n -> p c n", p=128)

        def load_x(b, c, lo_engine):
            piece(("x", b, c), xT_v[:, c, b * 512:(b + 1) * 512],
                  [t[:, c, b * 512:(b + 1) * 512] for t in xT], lo_engine=lo_engine)

        def load_wk(g, lo_engine="pool"):
            piece(("wk", g), wk_v[:, :, g * 128:(g + 1) * 128], [t[:, :] for t in wk], shape=C,
                  after=[("K", 2 * g - 1)] if g else [], lo_engine=lo_engine)

        def load_wq(g, h, lo_engine="pool"):
            n = HG * g + h
            piece(("wq", g, h), wq_v[:, :, n * 128:(n + 1) * 128], [t[:, h, :] for t in wq], shape=C,
                  after=[("Q", 2 * g - 1, h)] if g else [], lo_engine=lo_engine)

        def load_wo(g, h, lo_engine="pool"):
            n = HG * g + h
            old = (n - NWO) // HG
            piece(("wo", g, h), wo_v[:, n, :], [t[:, n % NWO, :] for t in wo],
                  after=[("W", 8 * old + 7)] if n >= NWO else [], lo_engine=lo_engine)

        def load_wv(p, k, lo_engine="pool"):
            piece(("wv", p, k), wv_v[:, 2 * k:2 * k + 2, p * 256:(p + 1) * 256],
                  [t[:, k * 512:(k + 1) * 512] for t in wv], shape=2,
                  after=[("Vp", p - 1, 7)] if p else [], lo_engine=lo_engine)

        def x_of(b):
            return [("lo", "x", b, c) for c in range(C)]

        def project_k(u):
            g, b = divmod(u, B)
            out, n, before = take("A")
            w = [[t[:, c * 128:(c + 1) * 128] for t in wk] for c in range(C)]
            x = [[t[:, c, b * 512:(b + 1) * 512] for t in xT] for c in range(C)]
            early = [(w[c][i], x[c][0], [("hi", "x", b, c)]) for c in range(C) for i in (0, 1)]
            late = [(w[c][0], x[c][1], [("lo", "x", b, c)]) for c in range(C)]
            products(out[:, :], early + late, before + [("lo", "wk", g)], ("K", u))
            split(out[:, :], kT[0], kT[1], ("kT", u),
                  [("K", u)] + ([("S", 4 * u - 1, HG - 1)] if u else []))
            give(n, ("lo", "kT", u))

        def project_q(u, h):
            g, b = divmod(u, B)
            out, n, before = take("A")
            passes(out[:, :], [([t[:, h, c * 128:(c + 1) * 128] for t in wq],
                                [t[:, c, b * 512:(b + 1) * 512] for t in xT]) for c in range(C)],
                   before + [("lo", "wq", g, h)], ("Q", u, h), each=x_of(b))
            split(out[:, :], qT[0][:, h, :], qT[1][:, h, :], ("qT", u, h),
                  [("Q", u, h)] + ([("S", 4 * u - 1, h)] if u else []))
            give(n, ("lo", "qT", u, h))

        def v_slot(p, tt):
            return (8 * p + tt) % NV

        def project_v(p, tt):
            out, n, before = take("A")
            old = 8 * p + tt - NV
            after = []
            if old >= 0:
                op_, ot = divmod(old, 8)
                after = [("V", 4 * (2 * (2 * op_ + 1) + ot // 4) + 3, 3)]
            passes(out[:, 0:256], [([t[:, c, tt * 128:(tt + 1) * 128] for t in xT],
                                    [t[:, c * 256:(c + 1) * 256] for t in wv]) for c in range(C)],
                   before + [("lo", "wv", p, 0), ("lo", "wv", p, 1)] + x_of(tt // 4), ("Vp", p, tt))
            s = v_slot(p, tt)
            split(out[:, 0:256], v[0][:, s, :], v[1][:, s, :], ("v", p, tt), [("Vp", p, tt)] + after)
            give(n, ("lo", "v", p, tt))

        def score(t, h):
            if t >= NT:
                return
            u, i = divmod(t, NI)
            w = 128 * (i + 1)
            out, n, before = take("S")
            passes(out[:, 0:w], [([x[:, h, i * 128:(i + 1) * 128] for x in qT], [x[:, 0:w] for x in kT])],
                   before + [("lo", "qT", u, h), ("lo", "kT", u)], ("S", t, h))
            maximum(t, h, out[:, 0:w], mask[:, 512 - w:512], [("S", t, h), "mask"])
            give(n, ("max", t, h))

        def maximum(t, h, s, more, waits):
            k = 4 * (t % 2) + h
            op("dve", lambda e: e.tensor_tensor_reduce(
                out=pr[:, k, 0:s.shape[-1]], in0=s, in1=more, scale=-SCALE, scalar=BIG, op0=ALU.add, op1=ALU.min,
                accum_out=mx[:, k:k + 1]), waits + ([("T", t - 2, (t - 2) % NI)] if t >= 2 else []), ("max", t, h))

        def score_first(t, h):
            u = t // NI
            out, n, before = take("S")
            o = out[:, :].rearrange("p (h s n) -> p h s n", h=2, s=2)
            for m in range(2):
                products(o[:, m, :, :], [(x[:, h + m, 0:128], kTs[:, :, 0:128], ()) for x in qT],
                         (before if m == 0 else []) + [("lo", "qT", u, h + m), ("lo", "kT", u)], ("S", t, h + m))
            k = 4 * (t % 2) + h
            op("dve", lambda e: e.tensor_tensor(
                out=pr[:, k:k + 2, 0:128], in0=o[:, :, 1, :],
                in1=mask[:, 384:512].rearrange("p (a n) -> p a n", a=1).to_broadcast([128, 2, 128]), op=ALU.add),
               [("S", t, h + 1), "mask"] + ([("T", t - 2, (t - 2) % NI)] if t >= 2 else []), ("masked", t, h))
            for m in range(2):
                maximum(t, h + m, o[:, m, 0, :], pr[:, k + m, 0:128], [("masked", t, h)])
            give(n, ("max", t, h + 1))

        def exponent(t, h):
            if t >= NT:
                return
            w = 128 * (t % NI + 1)
            k = 4 * (t % 2) + h
            op("act", lambda e: e.activation(
                pr[:, k, 0:w], pr[:, k, 0:w], ACT.Exp, bias=mx[:, k:k + 1], scale=-1.0,
                accum_out=rs[:, k:k + 1]), [("max", t, h)], ("exp", t, h))

        def normalise(t):
            if t >= NT:
                return
            w = 128 * (t % NI + 1)
            k0 = 4 * (t % 2)
            op("dve", lambda e: e.reciprocal(ri[:, k0:k0 + 4], rs[:, k0:k0 + 4]), [("exp", t, HG - 1)],
               ("ri", t))
            for h in range(HG):
                k = k0 + h
                p = pr[:, k, 0:w]
                if h < 1:
                    op("pool", lambda e, p=p, k=k: e.tensor_tensor(
                        out=p, in0=p, in1=ri[:, k:k + 1].to_broadcast([128, w]), op=ALU.mult),
                       [("ri", t)], ("p", t, h))
                else:
                    op("dve", lambda e, p=p, k=k: e.tensor_scalar(p, p, ri[:, k:k + 1], None, ALU.mult),
                       [("ri", t)], ("p", t, h))

        pt_at, pt_n = {}, [0]

        def turn(t, j):
            out, n, before = take("T")
            for h in range(HG):
                op("pe", lambda e, h=h: e.transpose(out[:, h * 128:(h + 1) * 128],
                                                    pr[:, 4 * (t % 2) + h, j * 128:(j + 1) * 128], ident[:, :]),
                   (before + ["ident"] if h == 0 else []) + [("p", t, h)], ("T", t, j) if h == HG - 1 else None)
            s = pt_n[0]
            pt_n[0] += 1
            pt_at[s] = (t, j)
            split(out[:, :], pT[0][:, s % NPT, :], pT[1][:, s % NPT, :], ("pT", t, j),
                  [("T", t, j)] + ([("V", *pt_at[s - NPT])] if s >= NPT else []))
            pt_at[t, j] = s % NPT
            give(n, ("lo", "pT", t, j))

        pv_bank = {}

        def weigh(t, j):
            u, i = divmod(t, NI)
            g, b = divmod(u, B)
            if j == 0:
                pv_bank[t] = take("A")
            out, n, before = pv_bank[t]
            s, k = v_slot(g // 2, 4 * b + j), pt_at[t, j]
            cols = slice((g % 2) * 128, (g % 2) * 128 + 128)
            passes(out[:, :], [([x[:, s, cols] for x in v], [x[:, k, :] for x in pT])],
                   (before if j == 0 else []) + [("lo", "pT", t, j), ("lo", "v", g // 2, 4 * b + j)],
                   ("V", t, j), j == 0, j == i)
            if j == i:
                split(out[:, :], oT[0][:, t % 2, :], oT[1][:, t % 2, :], ("oT", t),
                      [("V", t, i)] + ([("W", t - 2)] if t >= 2 else []))
                give(n, ("lo", "oT", t))

        wo_bank = {}

        def out_proj(t, h):
            u, i = divmod(t, NI)
            g, b = divmod(u, B)
            if h == 0:
                wo_bank[t] = take("A")
            out, n, before = wo_bank[t]
            s = (HG * g + h) % NWO
            passes(out[:, :], [([x[:, t % 2, h * 128:(h + 1) * 128] for x in oT], [x[:, s, :] for x in wo])],
                   (before if h == 0 else []) + [("lo", "oT", t), ("lo", "wo", g, h)],
                   ("W", t) if h == HG - 1 else None, h == 0, h == HG - 1)
            if h == HG - 1:
                k = 4 * b + i
                op("dve", lambda e: e.tensor_tensor(out=y[:, k, :], in0=out[:, :], in1=y[:, k, :], op=ALU.add),
                   [("W", t), ("y", g - 1, k) if g else "x"], ("y", g, k))
                give(n, ("y", g, k))

        def stats(k, name, waits):
            n = k % 4 + (4 if name[0] == "ln2" else 0)
            op("dve", lambda e: e.bn_stats(st[:, n, :], y[:, k, :]), waits, name + ("st",))
            op("dve", lambda e: e.bn_aggr(mv[:, n, :], st[:, n, :]), [name + ("st",)], name + ("mv",))
            op("pool", lambda e: e.tensor_scalar(vs[:, n:n + 1], mv[:, n, 1:2], EPS, None, ALU.add),
               [name + ("mv",)], name + ("vs",))
            op("pool", lambda e: e.tensor_tensor(out=rstd[:, n:n + 1], in0=vs[:, n:n + 1], in1=mhalf[:, :],
                                                 op=ALU.pow), [name + ("vs",), "mhalf"], name + ("rstd",))
            return mv[:, n, 0:1], rstd[:, n:n + 1]

        def apply(k, name, mean, r):
            op("dve", lambda e: e.tensor_scalar(y[:, k, :], y[:, k, :], mean, r, ALU.subtract, ALU.mult),
               [name + ("rstd",)], name)

        ln = {}

        def ffn_stats(k):
            ln[k] = stats(k, ("ln1", k), [("y", G - 1, k)])

        def ffn_apply(k):
            apply(k, ("ln1", k), *ln[k])

        def ffn_turn(k):
            out, n, before = take("T")
            for c in range(C):
                op("pe", lambda e, c=c: e.transpose(out[:, c * 128:(c + 1) * 128], y[:, k, c * 128:(c + 1) * 128],
                                                    ident[:, :]),
                   before + [("ln1", k)] if c == 0 else (), ("zt", k) if c == C - 1 else None)
            after = [("base", k - 4), ("R", k - 4)] if k >= 4 else [("Q", NU - 1, HG - 1)]
            split(out[:, :], zT[0][:, k % 4, :], zT[1][:, k % 4, :], ("zT", k), [("zt", k)] + after)
            give(n, ("lo", "zT", k))
            op("pool", lambda e: e.tensor_tensor(out=y[:, k, :], in0=y[:, k, :], in1=bb[:, :], op=ALU.add),
               [("zt", k), "bias"], ("zb", k))

        ffn_bank = {}

        def ffn_lhs(k):
            return [[t[:, k % 4, c * 128:(c + 1) * 128] for t in zT] for c in range(C)]

        def ffn_base(k, cs=range(C)):
            if cs[0] == 0:
                ffn_bank[k] = take("A")
            base, _, before = ffn_bank[k]
            lhs = ffn_lhs(k)
            passes(base[:, :], [(lhs[c], wb[c]) for c in cs], before + [("lo", "zT", k)], ("base", k),
                   first=cs[0] == 0, last=False, each=[("lo", "wb", c) for c in cs])

        def ffn_route(k):
            ra, n, before = take("S")
            products(ra[:, 0:272].rearrange("p (a n) -> p a n", a=2),
                     [(z, wras[:, :, c * 136:(c + 1) * 136], ()) for c, a in enumerate(ffn_lhs(k)) for z in a],
                     before + [("lo", "zT", k), ("lo", "wra")], ("R", k))
            ra_bank[k] = ra, n

        ra_bank = {}

        def ffn_sparsemax(k):
            ra, n = ra_bank[k]
            q = k % 2
            lg, so, cu, fk, w8 = (sp[:, q, 8 * m:8 * m + 8] for m in range(5))
            tau = sp[:, q, 40:41]
            name = ("sp", k)

            def chain(m, fn, *more):
                op("dve", fn, [*more, *([name + (m - 1,)] if m else [])], name + (m,))

            op("act", lambda e: e.activation(rl[:, q, :], ra[:, 136:272], ACT.Copy), [("R", k)], name + ("lo",))
            op("dve", lambda e: e.tensor_tensor(out=rl[:, q, :], in0=ra[:, 0:136], in1=rl[:, q, :], op=ALU.add),
               [name + ("lo",)], name + ("sum",))
            give(n, name + ("sum",))
            chain(0, lambda e: e.tensor_tensor(out=lg, in0=rl[:, q, 0:8], in1=br[:, :], op=ALU.add),
                  name + ("sum",), "bias")
            chain(1, lambda e: e.max(so, lg))
            chain(2, lambda e: e.tensor_tensor_scan(cu, ones8[:, :], so, -1.0, ALU.mult, ALU.add), "ones8")
            chain(3, lambda e: e.tensor_tensor_reduce(out=fk, in0=cu, in1=ik[:, :], scale=1.0, scalar=-BIG,
                                                      op0=ALU.mult, op1=ALU.max, accum_out=tau), "ik")
            chain(4, lambda e: e.tensor_scalar(w8, lg, tau, 0.0, ALU.subtract, ALU.max))
            chain(5, lambda e: e.tensor_tensor(
                out=hw[:, q, :].rearrange("p (a r) -> p a r", a=8),
                in0=rl[:, q, 8:136].rearrange("p (a r) -> p a r", a=8),
                in1=w8.rearrange("p (a r) -> p a r", r=1).to_broadcast([128, 8, 16]), op=ALU.mult))

        def ffn_experts(k):
            q = k % 2
            out, n, before = take("S")
            op("pe", lambda e: e.transpose(out[:, 0:128], hw[:, q, :], ident[:, :]), before + [("sp", k, 5)], ("ht", k))
            split(out[:, 0:128], hwT[0][:, q, :], hwT[1][:, q, :], ("hwT", k),
                  [("ht", k)] + ([("F", k - 2)] if k >= 2 else []))
            give(n, ("lo", "hwT", k))

        def ffn_sum(k):
            q = k % 2
            base, m, _ = ffn_bank[k]
            passes(base[:, :], [([t[:, q, :] for t in hwT], lb)], [("lo", "hwT", k), ("lo", "lb")], ("F", k), first=False)
            op("dve", lambda e: e.tensor_tensor(out=y[:, k, :], in0=base[:, :], in1=y[:, k, :], op=ALU.add),
               [("F", k), ("zb", k)], ("y2", k))
            give(m, ("y2", k))
            if k < 5:
                ffn_stats2(k)

        def ffn_stats2(k):
            ln[k] = stats(k, ("ln2", k), [("y2", k)])
            n = k % 4
            if k < 7:
                op("pool", lambda e: e.tensor_scalar(nmr[:, n:n + 1], ln[k][0], -1.0, ln[k][1], ALU.mult, ALU.mult),
                   [("ln2", k, "rstd")], ("nmr", k))

        def ffn_finish(k):
            n = k % 4
            if k < 7:
                op("act", lambda e: e.activation(y[:, k, :], y[:, k, :], ACT.Identity, bias=nmr[:, n:n + 1],
                                                 scale=ln[k][1]), [("nmr", k)], ("ln2", k))
            else:
                apply(k, ("ln2", k), *ln[k])
            op("sp", lambda e: e.dma_start(out_d[k * 128:(k + 1) * 128, :], y[:, k, :]), [("ln2", k)],
               ("out", k), dma="out")

        op("pool", lambda e: e.memset(mask[:, :], 0.0), mark="mask0")
        op("pool", lambda e: e.memset(ident[:, :], 0.0), mark="ident0")
        op("pool", lambda e: e.affine_select(out=mask[:, 384:512], in_=mask[:, 384:512], compare_op=ALU.is_ge,
                                             fill=-BIG, base=0, pattern=[[-1, 128]], channel_multiplier=1),
           ["mask0"], "mask")
        op("pool", lambda e: e.affine_select(out=ident[:, :], in_=ident[:, :], compare_op=ALU.not_equal, fill=1.0,
                                             base=0, pattern=[[-1, 128]], channel_multiplier=1), ["ident0"], "ident")
        op("pool", lambda e: e.memset(mhalf[:, :], -0.5), mark="mhalf")
        op("pool", lambda e: e.memset(ones8[:, :], 1.0), mark="ones8")
        for m in range(8):
            op("pool", lambda e, m=m: e.memset(ik[:, m:m + 1], 1.0 / (m + 1)), mark="ik")

        load_wk(0, "dve")
        for c in range(C):
            load_x(0, c, "dve")
        for h in range(HG):
            load_wq(0, h, "pool" if h % 2 else "dve")
        for k in range(2):
            load_wv(0, k, "dve" if k else "pool")
        for n in range(6):
            op("pe", lambda e: e.matmul(bank[4][:, 0:128], ident[:, :], ident[:, :], start=True, stop=True), ["ident"])
        project_k(0)
        load_x(1, 0, "pool")
        load_x(1, 1, "dve")
        project_q(0, 0)
        load_x(1, 2, "pool")
        load_x(1, 3, "dve")
        project_q(0, 1)
        load_wo(0, 0, "dve")
        project_q(0, 2)
        load_wo(0, 1, "pool")
        score_first(0, 0)
        exponent(0, 0)
        exponent(0, 1)
        project_q(0, 3)
        load_wo(0, 2, "dve")
        load_wo(0, 3, "pool")
        project_v(0, 0)
        score_first(0, 2)
        exponent(0, 2)
        exponent(0, 3)
        normalise(0)
        project_v(0, 1)
        project_v(0, 2)
        op("sp", lambda e: e.dma_start(bb[:, :], bb_d.rearrange("(a n) -> a n", a=1).to_broadcast([128, 512])),
           mark="bias", dma="b")
        op("sp", lambda e: e.dma_start(br[:, :], br_d.rearrange("(a n) -> a n", a=1).to_broadcast([128, 8])),
           mark="bias", dma="b")
        op("sp", lambda e: e.dma_start(y[:, :, :], x_d.rearrange("(k p) n -> p k n", p=128)), mark="x", dma="x")

        def loads(u, i):
            g, b = divmod(u, B)
            if b == 0 and i == 0 and g:
                load_wo(g, 2)
                load_wo(g, 3)
            if g == G - 1:
                if b == 0:
                    if i == 0:
                        load_wra()
                    if i in (1, 2):
                        load_wb(2 * i - 2)
                        load_wb(2 * i - 1)
                    if i == 3:
                        load_lb()
                return
            if b == 0:
                if i in (1, 2):
                    load_wo(g + 1, i - 1)
            else:
                if i == 0:
                    load_wk(g + 1)
                    load_wq(g + 1, 0)
                if i == 1:
                    load_wq(g + 1, 1)
                    load_wq(g + 1, 2)
                if i == 2:
                    load_wq(g + 1, 3)
                if u % 4 == 1 and i < 2 and u // 4 < 3:
                    load_wv(u // 4 + 1, i)

        def v_tile(u, i):
            p, r = divmod(u, 4)
            if r == 0:
                return p, 4 + i
            if p < 3:
                return {(1, 3): (p + 1, 0), (2, 3): (p + 1, 1), (3, 1): (p + 1, 2), (3, 3): (p + 1, 3)}.get((r, i))

        def load_wra():
            piece(("wra",), wra_v, wra, cols=544, shape=C, after=[("V", 47, 3)])

        def load_wb(c):
            piece(("wb", c), wb_v[:, c, :], wb[c], after=[("Vp", 3, 7) if c < 2 else ("W", 55)])

        def load_lb():
            piece(("lb",), lb_d, lb, after=[("K", NU - 1)])

        for t in range(NT):
            u, i = divmod(t, NI)
            burst = i == NI - 1 and u + 1 < NU
            late = u == NU - 1
            tv = v_tile(u, i)
            fill = [(out_proj, t - 1, h) for h in range(HG)] if t else [(project_v, 0, 3)]

            def filler():
                if fill:
                    f, *a = fill.pop(0)
                    f(*a)

            if burst:
                project_k(u + 1)
                turn(t, 0)
                turn(t, 1)
                if u == NU - 2:
                    ffn_stats(0)
                    ffn_stats(1)
                project_q(u + 1, 0)
                weigh(t, 0)
                turn(t, 2)
                weigh(t, 1)
                project_q(u + 1, 1)
                turn(t, 3)
                weigh(t, 2)
                project_q(u + 1, 2)
                weigh(t, 3)
                if u == NU - 2:
                    ffn_apply(0)
                project_q(u + 1, 3)
                if tv:
                    filler()
                for h in (0, 2):
                    if h:
                        filler()
                    score_first(t + 1, h)
                    exponent(t + 1, h)
                    exponent(t + 1, h + 1)
                normalise(t + 1)
                if tv:
                    project_v(*tv)
                if u == NU - 2:
                    filler()
                    ffn_turn(0)
                while fill:
                    filler()
            elif t == NT - 1:
                turn(t, 0)
                filler()
                filler()
                turn(t, 1)
                ffn_sum(i - 1)
                turn(t, 2)
                weigh(t, 0)
                ffn_route(i)
                ffn_sparsemax(i)
                turn(t, 3)
                weigh(t, 1)
                filler()
                weigh(t, 2)
                filler()
                weigh(t, 3)
                ffn_apply(i + 1)
                ffn_stats(i + 2)
                ffn_base(i)
                ffn_turn(i + 1)
                ffn_finish(i - 1)
                ffn_experts(i)
            else:
                score(t + 1, 0)
                turn(t, 0)
                if late and i:
                    filler()
                if i >= 1:
                    turn(t, 1)
                exponent(t + 1, 0)
                score(t + 1, 1)
                filler()
                if late and i:
                    ffn_sum(i - 1)
                if i >= 2:
                    turn(t, 2)
                exponent(t + 1, 1)
                score(t + 1, 2)
                exponent(t + 1, 2)
                score(t + 1, 3)
                exponent(t + 1, 3)
                normalise(t + 1)
                for j in range(i + 1):
                    if j:
                        filler()
                    weigh(t, j)
                    if late and j == min(1, i):
                        ffn_route(i)
                        ffn_apply(i + 1)
                        ffn_sparsemax(i)
                if tv:
                    project_v(*tv)
                while fill:
                    filler()
                if late:
                    ffn_stats(i + 2)
                    ffn_base(i)
                    ffn_turn(i + 1)
                    if i:
                        ffn_finish(i - 1)
                    ffn_experts(i)
            loads(u, i)
        ffn_apply(5)
        ffn_stats(6)
        for h in range(HG):
            out_proj(NT - 1, h)
        ffn_apply(6)
        ffn_stats(7)
        ffn_route(4)
        ffn_turn(5)
        ffn_sparsemax(4)
        ffn_sum(3)
        ffn_apply(7)
        ffn_base(4)
        ffn_turn(6)
        ffn_route(5)
        ffn_experts(4)
        ffn_sparsemax(5)
        ffn_base(5)
        ffn_turn(7)
        ffn_finish(3)
        ffn_sum(4)
        ffn_route(6)
        ffn_experts(5)
        ffn_sparsemax(6)
        ffn_base(6)
        ffn_route(7)
        ffn_experts(6)
        ffn_sparsemax(7)
        ffn_sum(5)
        ffn_finish(4)
        ffn_base(7, range(3))
        ffn_experts(7)
        ffn_sum(6)
        ffn_base(7, range(3, C))
        ffn_stats2(5)
        ffn_finish(5)
        ffn_stats2(6)
        ffn_finish(6)
        ffn_sum(7)
        ffn_stats2(7)
        ffn_finish(7)

        block = ctx.enter_context(nc.Block())

        @block.sync
        def _(eng):
            play("sp", eng)
            eng.wait_ge(s_out, 16 * 8)

        @block.gpsimd
        def _(eng):
            play("pool", eng)

        @block.scalar
        def _(eng):
            play("act", eng)

        @block.vector
        def _(eng):
            play("dve", eng)

        @block.tensor
        def _(eng):
            play("pe", eng)


def kernel(L0_attn_hidden_states, L0_attn_Wq, L0_attn_Wk, L0_attn_Wv, L0_attn_Wo, L0_ffn_W_base, L0_ffn_b_base,
           L0_ffn_W_router, L0_ffn_b_router, L0_ffn_lora_A, L0_ffn_lora_B):
    import concourse.bacc as bacc
    from concourse.bass_utils import run_bass_kernel_spmd

    x = np.asarray(L0_attn_hidden_states).reshape(1024, 512)
    router = np.asarray(L0_ffn_W_router).T
    lora_a = np.asarray(L0_ffn_lora_A).transpose(1, 0, 2).reshape(512, 128)
    arrays = {
        "xT": x.T, "x": x,
        "wq": L0_attn_Wq, "wk": L0_attn_Wk, "wv": L0_attn_Wv, "wo": L0_attn_Wo,
        "wb": np.asarray(L0_ffn_W_base).T, "wra": np.concatenate([router, lora_a], axis=1),
        "lb": np.asarray(L0_ffn_lora_B).reshape(128, 512),
        "bb": L0_ffn_b_base, "br": L0_ffn_b_router,
    }
    arrays = {n: np.ascontiguousarray(a) for n, a in arrays.items()}
    nc = bacc.Bacc("TRN2", target_bir_lowering=False, num_devices=1)
    args = [nc.dram_tensor(f"in_{n}", a.shape, mybir.dt.from_np(a.dtype), kind="ExternalInput").ap()
            for n, a in arrays.items()]
    args.append(nc.dram_tensor("out", (1024, 512), mybir.dt.float32, kind="ExternalOutput").ap())
    post_ln_block(nc, *args)
    r = run_bass_kernel_spmd(nc, [{f"in_{n}": a for n, a in arrays.items()}], core_ids=[0])
    return r.results[0]["out"].reshape(2, 512, 512)
```
